# Optimizing a Trainium2 kernel written in Bass

```python
import numpy as np
import jax
import jax.numpy as jnp

def _softmax(x, axis=-1):
    return jax.nn.softmax(x, axis=axis)

def _gelu(x):
    return jax.nn.gelu(x, approximate=True)

def _silu(x):
    return jax.nn.silu(x)

def _sigmoid(x):
    return jax.nn.sigmoid(x)

def _layernorm(x, axis=-1, eps=1e-05):
    m = jnp.mean(x, axis=axis, keepdims=True)
    v = jnp.var(x, axis=axis, keepdims=True)
    return (x - m) / jnp.sqrt(v + eps)

def _scatter_add(tgt, idx, src, axis=0):
    return tgt.at[idx].add(src)

def _segment_sum(src, seg, n):
    return jax.ops.segment_sum(src, seg, n)
kernel_name = 'mk_dlrm_tower_d1_rec_r8_c2ff87'

def setup_inputs(seed: int=0):
    np.random.seed(seed)
    _w = jnp.asarray

    def _rec_inputs():
        import jax
        import jax.numpy as jnp
        _tk = jax.random.key(seed)
        dense_ctx = jax.random.normal(jax.random.fold_in(_tk, 190), (2048, 16), jnp.float32)
        ids = jnp.stack([jax.random.randint(jax.random.fold_in(_tk, 200 + f), (2048,), 0, v, jnp.int32) for f, v in enumerate([125000, 12500, 1250, 1250, 12500, 12500, 12500, 1250, 1250, 12500, 1250, 1250, 1250, 12500, 1000, 12500, 1250, 12500, 1000, 1250, 1000, 1250, 1000, 1000, 1250, 1250, 1000])], axis=1)
        tbl_0 = 0.05 * jax.random.normal(jax.random.fold_in(_tk, 500 + 0), (125000, 128), jnp.float32)
        tbl_1 = 0.05 * jax.random.normal(jax.random.fold_in(_tk, 500 + 1), (12500, 128), jnp.float32)
        tbl_2 = 0.05 * jax.random.normal(jax.random.fold_in(_tk, 500 + 2), (1250, 128), jnp.float32)
        tbl_3 = 0.05 * jax.random.normal(jax.random.fold_in(_tk, 500 + 3), (1250, 128), jnp.float32)
        tbl_4 = 0.05 * jax.random.normal(jax.random.fold_in(_tk, 500 + 4), (12500, 128), jnp.float32)
        tbl_5 = 0.05 * jax.random.normal(jax.random.fold_in(_tk, 500 + 5), (12500, 128), jnp.float32)
        tbl_6 = 0.05 * jax.random.normal(jax.random.fold_in(_tk, 500 + 6), (12500, 128), jnp.float32)
        tbl_7 = 0.05 * jax.random.normal(jax.random.fold_in(_tk, 500 + 7), (1250, 128), jnp.float32)
        tbl_8 = 0.05 * jax.random.normal(jax.random.fold_in(_tk, 500 + 8), (1250, 128), jnp.float32)
        tbl_9 = 0.05 * jax.random.normal(jax.random.fold_in(_tk, 500 + 9), (12500, 128), jnp.float32)
        tbl_10 = 0.05 * jax.random.normal(jax.random.fold_in(_tk, 500 + 10), (1250, 128), jnp.float32)
        tbl_11 = 0.05 * jax.random.normal(jax.random.fold_in(_tk, 500 + 11), (1250, 128), jnp.float32)
        tbl_12 = 0.05 * jax.random.normal(jax.random.fold_in(_tk, 500 + 12), (1250, 128), jnp.float32)
        tbl_13 = 0.05 * jax.random.normal(jax.random.fold_in(_tk, 500 + 13), (12500, 128), jnp.float32)
        tbl_14 = 0.05 * jax.random.normal(jax.random.fold_in(_tk, 500 + 14), (1000, 128), jnp.float32)
        tbl_15 = 0.05 * jax.random.normal(jax.random.fold_in(_tk, 500 + 15), (12500, 128), jnp.float32)
        tbl_16 = 0.05 * jax.random.normal(jax.random.fold_in(_tk, 500 + 16), (1250, 128), jnp.float32)
        tbl_17 = 0.05 * jax.random.normal(jax.random.fold_in(_tk, 500 + 17), (12500, 128), jnp.float32)
        tbl_18 = 0.05 * jax.random.normal(jax.random.fold_in(_tk, 500 + 18), (1000, 128), jnp.float32)
        tbl_19 = 0.05 * jax.random.normal(jax.random.fold_in(_tk, 500 + 19), (1250, 128), jnp.float32)
        tbl_20 = 0.05 * jax.random.normal(jax.random.fold_in(_tk, 500 + 20), (1000, 128), jnp.float32)
        tbl_21 = 0.05 * jax.random.normal(jax.random.fold_in(_tk, 500 + 21), (1250, 128), jnp.float32)
        tbl_22 = 0.05 * jax.random.normal(jax.random.fold_in(_tk, 500 + 22), (1000, 128), jnp.float32)
        tbl_23 = 0.05 * jax.random.normal(jax.random.fold_in(_tk, 500 + 23), (1000, 128), jnp.float32)
        tbl_24 = 0.05 * jax.random.normal(jax.random.fold_in(_tk, 500 + 24), (1250, 128), jnp.float32)
        tbl_25 = 0.05 * jax.random.normal(jax.random.fold_in(_tk, 500 + 25), (1250, 128), jnp.float32)
        tbl_26 = 0.05 * jax.random.normal(jax.random.fold_in(_tk, 500 + 26), (1000, 128), jnp.float32)
        _rk = jax.random.fold_in(_tk, 7)
        W_top1 = 0.0521996 * jax.random.normal(jax.random.fold_in(_tk, 801), (367, 512), jnp.float32)
        W_top2 = 0.0441942 * jax.random.normal(jax.random.fold_in(_tk, 802), (512, 256), jnp.float32)
        W_top3 = 0.0625 * jax.random.normal(jax.random.fold_in(_tk, 803), (256, 1), jnp.float32)
        b_top1 = jnp.zeros((512,), jnp.float32)
        b_top2 = jnp.zeros((256,), jnp.float32)
        return (dense_ctx, ids, tbl_0, tbl_1, tbl_2, tbl_3, tbl_4, tbl_5, tbl_6, tbl_7, tbl_8, tbl_9, tbl_10, tbl_11, tbl_12, tbl_13, tbl_14, tbl_15, tbl_16, tbl_17, tbl_18, tbl_19, tbl_20, tbl_21, tbl_22, tbl_23, tbl_24, tbl_25, tbl_26, W_top1, b_top1, W_top2, b_top2, W_top3)
    dense_ctx, ids, tbl_0, tbl_1, tbl_2, tbl_3, tbl_4, tbl_5, tbl_6, tbl_7, tbl_8, tbl_9, tbl_10, tbl_11, tbl_12, tbl_13, tbl_14, tbl_15, tbl_16, tbl_17, tbl_18, tbl_19, tbl_20, tbl_21, tbl_22, tbl_23, tbl_24, tbl_25, tbl_26, W_top1, b_top1, W_top2, b_top2, W_top3 = _rec_inputs()

    def _L0_rec_setup():
        import jax, jax.numpy as jnp
        import numpy as np
        B, F, D = (2048, 27, 128)
        _TRIL_I, _TRIL_J = np.tril_indices(F, k=-1)
        key = jax.random.key(seed)
        features = jax.random.normal(key, (B, F, D), dtype=jnp.float32)
        return {'features': features}
    _L0_rec_all = _L0_rec_setup()
    _L0_rec_in = {k: v for k, v in _L0_rec_all.items() if k in ()}
    del _L0_rec_all
    return {'dense_ctx': dense_ctx, 'ids': ids, 'tbl_0': tbl_0, 'tbl_1': tbl_1, 'tbl_2': tbl_2, 'tbl_3': tbl_3, 'tbl_4': tbl_4, 'tbl_5': tbl_5, 'tbl_6': tbl_6, 'tbl_7': tbl_7, 'tbl_8': tbl_8, 'tbl_9': tbl_9, 'tbl_10': tbl_10, 'tbl_11': tbl_11, 'tbl_12': tbl_12, 'tbl_13': tbl_13, 'tbl_14': tbl_14, 'tbl_15': tbl_15, 'tbl_16': tbl_16, 'tbl_17': tbl_17, 'tbl_18': tbl_18, 'tbl_19': tbl_19, 'tbl_20': tbl_20, 'tbl_21': tbl_21, 'tbl_22': tbl_22, 'tbl_23': tbl_23, 'tbl_24': tbl_24, 'tbl_25': tbl_25, 'tbl_26': tbl_26, 'W_top1': W_top1, 'b_top1': b_top1, 'W_top2': W_top2, 'b_top2': b_top2, 'W_top3': W_top3}

def reference(dense_ctx, ids, tbl_0, tbl_1, tbl_2, tbl_3, tbl_4, tbl_5, tbl_6, tbl_7, tbl_8, tbl_9, tbl_10, tbl_11, tbl_12, tbl_13, tbl_14, tbl_15, tbl_16, tbl_17, tbl_18, tbl_19, tbl_20, tbl_21, tbl_22, tbl_23, tbl_24, tbl_25, tbl_26, W_top1, b_top1, W_top2, b_top2, W_top3):
    import jax
    import jax.numpy as jnp

    def _L0_rec_ref(features):
        import jax, jax.numpy as jnp
        import numpy as np
        B, F, D = (2048, 27, 128)
        _TRIL_I, _TRIL_J = np.tril_indices(F, k=-1)
        xactions = jnp.einsum('bfd,bgd->bfg', features, features)
        activations = xactions[:, _TRIL_I, _TRIL_J]
        return activations
    e = jnp.stack([tbl_0[ids[:, 0]], tbl_1[ids[:, 1]], tbl_2[ids[:, 2]], tbl_3[ids[:, 3]], tbl_4[ids[:, 4]], tbl_5[ids[:, 5]], tbl_6[ids[:, 6]], tbl_7[ids[:, 7]], tbl_8[ids[:, 8]], tbl_9[ids[:, 9]], tbl_10[ids[:, 10]], tbl_11[ids[:, 11]], tbl_12[ids[:, 12]], tbl_13[ids[:, 13]], tbl_14[ids[:, 14]], tbl_15[ids[:, 15]], tbl_16[ids[:, 16]], tbl_17[ids[:, 17]], tbl_18[ids[:, 18]], tbl_19[ids[:, 19]], tbl_20[ids[:, 20]], tbl_21[ids[:, 21]], tbl_22[ids[:, 22]], tbl_23[ids[:, 23]], tbl_24[ids[:, 24]], tbl_25[ids[:, 25]], tbl_26[ids[:, 26]]], axis=1)
    z = _L0_rec_ref(e)
    z = z.reshape(z.shape[0], -1)
    h = jnp.concatenate([z, dense_ctx], axis=1)
    h = jnp.maximum(h @ W_top1 + b_top1, 0.0)
    h = jnp.maximum(h @ W_top2 + b_top2, 0.0)
    y = h @ W_top3
    return y

_drawn_inputs = setup_inputs


def setup_inputs(seed=0):
    import zlib

    import numpy as np

    out = dict(_drawn_inputs(seed))
    spreads = {'b_top1': (0.0, 0.1), 'b_top2': (0.0, 0.1)}
    factors = {}
    for name, (base, spread) in spreads.items():
        noise = np.random.default_rng([zlib.crc32(name.encode()), seed]).standard_normal(out[name].shape)
        drawn = base * np.exp(spread * noise) if base else spread * noise
        out[name] = jnp.asarray(drawn.astype(out[name].dtype))
    for name, factor in factors.items():
        out[name] = (out[name] * factor).astype(out[name].dtype)
    return out
```

```python
from contextlib import ExitStack

import numpy as np

import concourse.bass as bass
from concourse import mybir

F32 = mybir.dt.float32
F32R = mybir.dt.float32r
I32 = mybir.dt.int32
ALU = mybir.AluOpType
ACT = mybir.ActivationFunctionType

P = 128
BATCH = 2048
DIM = 128
NF = 27
ROWS = [125000, 12500, 1250, 1250, 12500, 12500, 12500, 1250, 1250, 12500, 1250, 1250, 1250, 12500,
        1000, 12500, 1250, 12500, 1000, 1250, 1000, 1250, 1000, 1000, 1250, 1250, 1000]
N_SELECTED = 9
SELECTED = sorted(sorted(range(NF), key=lambda f: ROWS[f])[:N_SELECTED], key=lambda f: ROWS[f])
GATHERED = [f for f in range(NF) if f not in SELECTED]
NG = len(GATHERED)
ORDER = GATHERED + SELECTED

TILE = 128
TILES = 2
CHUNK = TILE * TILES
CHUNKS = BATCH // CHUNK
RP = 125
BLOCKS = [ROWS[f] // RP for f in SELECTED]
BLOCK_AT = [sum(BLOCKS[:i]) for i in range(N_SELECTED)]
HALVES = 2 * N_SELECTED
SETS = 3
SET_BLOCKS = max(BLOCKS) // 2
STAGES = 5

SLOT = 32
QUAD = 4
GROUP = 32
GROUPS = TILE // GROUP
TURNS = [(s, min(4, NG - s)) for s in range(0, NG, 4)]
NT = len(TURNS)
PAIRS = NF * (NF - 1) // 2
DENSE = 16
H1, H2 = 512, 256
N1, N2 = H1 // P, H2 // P
CONTRACT = PAIRS + DENSE
KC = -(-CONTRACT // P)

SECOND_HALF = [("layer1", 0), ("turn", 0), ("product", 0), ("turn", 1), ("layer1", 1), ("turn", 2),
               ("product", 1), ("turn", 3), ("product", 2), ("turn", 4), ("layer2", 0), ("product", 3),
               ("layer3", 0), ("product", 4), ("product", 5), ("product", 6), ("product", 7)]

assert NT <= 5 and all(ROWS[f] % RP == 0 and ROWS[f] // RP % 2 == 0 for f in SELECTED)


def packed_rows():
    return [(f, g) for g in range(NF - 1) for f in range(g + 1, NF)]


def packing():
    runs, at = [], 0
    for g in range(NF - 1):
        f = g + 1
        while f < NF:
            n = min(NF - f, P - at % P)
            runs.append((g, f, n, at // P, at % P))
            f, at = f + n, at + n
    return runs


RUNS = packing()
REPACK = 16 * (len(RUNS) + 1)


def dlrm_program(nc, ids_gathered, ids_selected, tables, dense_t, w1, b1, w2, b2, w3, y):
    with ExitStack() as ctx:
        def sb(name, shape, dt=F32):
            return ctx.enter_context(nc.sbuf_tensor(name, shape, dt))

        def ps(name, shape):
            return ctx.enter_context(nc.psum_tensor(name, shape, F32))

        def sem(name):
            return ctx.enter_context(nc.semaphore(name))

        ids_all = sb("ids_all", [P, BATCH // P * NG], I32)
        ids_now = sb("ids_now", [P, TILES, NG], I32)
        gathered = sb("gathered", [P, TILES, NG, DIM])
        ids_rep = sb("ids_rep", [P, N_SELECTED, CHUNK], I32)
        table_hi = sb("table_hi", [RP, sum(BLOCKS), DIM], F32R)
        table_lo = sb("table_lo", [RP, sum(BLOCKS), DIM], F32R)
        row_id = sb("row_id", [RP, sum(BLOCKS)])
        one_hot = sb("one_hot", [RP, SETS, SET_BLOCKS, CHUNK], F32R)
        feats = sb("feats", [P, CHUNK, SLOT])
        blocks = sb("blocks", [P, NF - 1, CHUNK])
        raw = blocks[:].rearrange("p g s -> p (g s)")
        packed = sb("packed", [P, KC, CHUNK])
        w1_sb = sb("w1_sb", [P, KC, H1])
        w2_sb = sb("w2_sb", [P, N1, H2])
        w3_sb = sb("w3_sb", [P, N2])
        b1_sb = sb("b1_sb", [P, N1])
        b2_sb = sb("b2_sb", [P, N2])
        h1 = sb("h1", [P, N1, CHUNK])
        h2 = sb("h2", [P, N2, CHUNK])
        y_sb = sb("y_sb", [P, BATCH // TILE])
        ident = sb("ident", [P, P])

        ps_t = ps("ps_t", [P, 4, TILE])
        ps_s = ps("ps_s", [P, 2, 512])
        ps_g = ps("ps_g", [P, 2, 2, 512])
        ps_m = ps("ps_m", [P, 2, CHUNK])

        ids_loaded = sem("ids_loaded")
        ids_staged = sem("ids_staged")
        tiles_begun = sem("tiles_begun")
        rows_gathered = [sem(f"rows_gathered{j}") for j in range(TILES)]
        ids_rep_loaded = sem("ids_rep_loaded")
        raw_loaded = [sem(f"raw_loaded{i}") for i in range(STAGES)]
        weights_loaded = sem("weights_loaded")
        hi_made = sem("hi_made")
        lo_made = sem("lo_made")
        row_ids_made = sem("row_ids_made")
        ident_zeroed = sem("ident_zeroed")
        ident_made = sem("ident_made")
        pads_zeroed = sem("pads_zeroed")
        one_hot_made = sem("one_hot_made")
        one_hot_used = sem("one_hot_used")
        selected_copied = sem("selected_copied")
        turned = sem("turned")
        turned_copied = sem("turned_copied")
        products_made = sem("products_made")
        blocks_by_act = sem("blocks_by_act")
        blocks_by_dve = sem("blocks_by_dve")
        packed_ready = sem("packed_ready")
        l1_made = sem("l1_made")
        h1_made = sem("h1_made")
        l2_made = sem("l2_made")
        h2_made = sem("h2_made")
        l3_made = sem("l3_made")
        y_made = sem("y_made")
        y_stored = sem("y_stored")

        def at_least(eng, semaphore, value):
            if not isinstance(value, int) or value > 0:
                eng.wait_ge(semaphore, value)

        block = ctx.enter_context(nc.Block())

        @block.sync
        def _(sp):
            def load_ids_rep(k):
                src = ids_selected[:, bass.ds(k * CHUNK, CHUNK)]
                sp.dma_start(ids_rep[:], src.partition_broadcast(P)).then_inc(ids_rep_loaded, 16)

            def pack(k):
                at_least(sp, l1_made, 2 * k)
                sp.dma_start(packed[PAIRS % P:PAIRS % P + DENSE, KC - 1, :],
                             dense_t[:, bass.ds(k * CHUNK, CHUNK)]).then_inc(packed_ready, 16)
                sp.wait_ge(blocks_by_act, TILES * GROUPS * (k + 1))
                sp.wait_ge(blocks_by_dve, TILES * GROUPS * (k + 1))
                for g, f, n, c, p in RUNS:
                    sp.dma_start(packed[p:p + n, c, :], blocks[f:f + n, g, :]).then_inc(packed_ready, 16)

            sp.dma_start(ids_all[:], ids_gathered).then_inc(ids_loaded, 16)
            load_ids_rep(0)
            for i, f in enumerate(SELECTED):
                if i >= STAGES:
                    sp.wait_ge(lo_made, i - STAGES + 1)
                sp.dma_start(raw[0:RP, (i % STAGES) * max(BLOCKS) * DIM:][:, 0:BLOCKS[i] * DIM],
                             tables[f].rearrange("(p b) d -> p (b d)", p=RP)).then_inc(raw_loaded[i % STAGES], 16)
            for c in range(KC):
                n = min(P, CONTRACT - c * P)
                sp.dma_start(w1_sb[0:n, c, :], w1[c * P:c * P + n, :]).then_inc(weights_loaded, 16)
            sp.dma_start(w2_sb[:], w2.rearrange("(c p) n -> p c n", p=P)).then_inc(weights_loaded, 16)
            sp.dma_start(w3_sb[:], w3).then_inc(weights_loaded, 16)
            sp.dma_start(b1_sb[:], b1).then_inc(weights_loaded, 16)
            sp.dma_start(b2_sb[:], b2).then_inc(weights_loaded, 16)

            sp.wait_ge(one_hot_made, HALVES)
            load_ids_rep(1)
            pack(0)
            with sp.Fori(1, CHUNKS - 1) as k:
                sp.wait_ge(one_hot_made, HALVES * (k + 1))
                load_ids_rep(k + 1)
                pack(k)
            pack(CHUNKS - 1)
            sp.wait_ge(y_made, 1 + CHUNKS)
            sp.dma_start(y, y_sb[:]).then_inc(y_stored, 16)
            sp.wait_ge(y_stored, 16)

        @block.gpsimd
        def _(pool):
            pool.memset(ident[:], 0.0).then_inc(ident_zeroed, 1)
            pool.wait_ge(ident_zeroed, 1)
            pool.affine_select(out=ident[:], in_=ident[:], compare_op=ALU.not_equal, fill=1.0, base=0,
                               pattern=[[-1, P]], channel_multiplier=1).then_inc(ident_made, 1)
            for at, n in zip(BLOCK_AT, BLOCKS):
                pool.iota(row_id[:, at:at + n], [[1, n]], base=0, channel_multiplier=n,
                          allow_small_or_imprecise_dtypes=True).then_inc(row_ids_made, 1)
            pool.wait_ge(ids_loaded, 16)

            def gather(k):
                for j in range(TILES):
                    at_least(pool, turned, TILES * NT * (k - 1) + NT * (j + 1))
                    pool.tensor_copy(ids_now[:, j, :], ids_all[:, bass.ds((k * TILES + j) * NG, NG)]).then_inc(ids_staged, 1)
                    pool.wait_ge(ids_staged, TILES * k + j + 1)
                    pool.sem_inc(tiles_begun)
                    for s, f in enumerate(GATHERED):
                        pool.indirect_dma_start(
                            gathered[:, j, s, :], None, tables[f],
                            bass.IndirectOffsetOnAxis(ids_now[:, j, s:s + 1], 0)).then_inc(rows_gathered[j], 16)

            gather(0)
            with pool.Fori(1, CHUNKS) as k:
                gather(k)

        @block.tensor
        def _(pe):
            def select(k, i):
                if i == 0:
                    at_least(pe, selected_copied, N_SELECTED * k)
                elif i >= 2:
                    pe.wait_ge(selected_copied, N_SELECTED * k + i - 1)
                for h in range(2):
                    pe.wait_ge(one_hot_made, HALVES * k + 2 * i + h + 1)
                    n = BLOCKS[i] // 2
                    for b in range(n):
                        at = BLOCK_AT[i] + h * n + b
                        picks = one_hot[:, (2 * i + h) % SETS, b, :]
                        pe.matmul(ps_s[:, i % 2, 0:CHUNK], table_hi[:, at, :], picks, start=(h + b == 0), stop=False)
                        mm = pe.matmul(ps_s[:, i % 2, 0:CHUNK], table_lo[:, at, :], picks, start=False,
                                       stop=(h == 1 and b == n - 1))
                    mm.then_inc(one_hot_used, 1)

            def turn(k, j, i):
                first, n = TURNS[i]
                if i == 0:
                    pe.wait_ge(rows_gathered[j], 16 * NG * (k + 1))
                at_least(pe, turned_copied, TILES * NT * k + NT * j + i)
                for s in range(n):
                    mm = pe.transpose(ps_t[:, s, :], gathered[:, j, first + s, :], ident[:])
                mm.then_inc(turned, 1)

            def product(k, j, q):
                if q == 0:
                    pe.wait_ge(turned_copied, TILES * NT * k + NT * (j + 1))
                if q == 0 and j == 0:
                    pe.wait_ge(selected_copied, N_SELECTED * (k + 1))
                n = GROUPS * j + q
                at_least(pe, blocks_by_act, TILES * GROUPS * k + n - 1)
                at_least(pe, blocks_by_dve, TILES * GROUPS * k + n - 1)
                for u in range(GROUP // QUAD):
                    s0 = j * TILE + q * GROUP + u * QUAD
                    four = feats[:, s0:s0 + QUAD, :]
                    out = ps_g[:, n % 2, u // 4, (u % 4) * QUAD * (NF - 1):(u % 4 + 1) * QUAD * (NF - 1)]
                    mm = pe.matmul(out, four.rearrange("p s f -> p (s f)"), four[:, :, 0:NF - 1],
                                   start=True, stop=True)
                mm.then_inc(products_made, 1)

            def layer1(m, half):
                if half == 0:
                    pe.wait_ge(packed_ready, REPACK * (m + 1))
                    pe.wait_ge(y_made, 1 + m)
                else:
                    pe.wait_ge(h1_made, N1 * m + N1 // 2)
                for n in range(2):
                    out = 2 * half + n
                    for c in range(KC):
                        kk = min(P, CONTRACT - c * P)
                        mm = pe.matmul(ps_m[:, n, :], w1_sb[0:kk, c, out * P:(out + 1) * P],
                                       packed[0:kk, c, :], start=(c == 0), stop=(c == KC - 1))
                mm.then_inc(l1_made, 1)

            def layer2(m):
                pe.wait_ge(h1_made, N1 * (m + 1))
                for n in range(N2):
                    for c in range(N1):
                        mm = pe.matmul(ps_m[:, n, :], w2_sb[:, c, n * P:(n + 1) * P], h1[:, c, :],
                                       start=(c == 0), stop=(c == N1 - 1))
                mm.then_inc(l2_made, 1)

            def layer3(m):
                pe.wait_ge(h2_made, N2 * (m + 1))
                for j in range(TILES):
                    for c in range(N2):
                        mm = pe.matmul(ps_m[:, 0, j:j + 1], h2[:, c, j * TILE:(j + 1) * TILE],
                                       w3_sb[:, c:c + 1], start=(c == 0), stop=(c == N2 - 1))
                mm.then_inc(l3_made, 1)

            def turn_of_loop(k, dense):
                for i in range(N_SELECTED):
                    select(k, i)
                    if i < NT:
                        turn(k, 0, i)
                for kind, i in SECOND_HALF:
                    if kind == "turn":
                        turn(k, 1, i)
                    if kind == "product":
                        product(k, i // GROUPS, i % GROUPS)
                    if kind == "layer1" and dense:
                        layer1(k - 1, i)
                    if kind == "layer2" and dense:
                        layer2(k - 1)
                    if kind == "layer3" and dense:
                        layer3(k - 1)

            pe.sem_inc(l2_made)
            pe.sem_inc(l3_made)
            pe.wait_ge(ident_made, 1)
            pe.wait_ge(hi_made, N_SELECTED)
            pe.wait_ge(lo_made, N_SELECTED)
            pe.wait_ge(pads_zeroed, 1)
            turn_of_loop(0, False)
            pe.wait_ge(weights_loaded, 16 * (KC + 4))
            with pe.Fori(1, CHUNKS) as k:
                turn_of_loop(k, True)
            layer1(CHUNKS - 1, 0)
            layer1(CHUNKS - 1, 1)
            layer2(CHUNKS - 1)
            layer3(CHUNKS - 1)

        def copy_blocks(eng, copy, k, n, samples, done):
            if n == 0:
                at_least(eng, packed_ready, REPACK * k)
            eng.wait_ge(products_made, TILES * GROUPS * k + n + 1)
            for s in samples:
                wide = ps_g[SLOT * s:SLOT * s + NF, n % 2, :, 0:4 * QUAD * (NF - 1)]
                src = wide.rearrange("p b (u t g) -> p b u t g", u=4, t=QUAD)[:, :, :, s, :]
                dst = blocks[0:NF, :, n * GROUP:(n + 1) * GROUP].rearrange(
                    "p g (b u t) -> p b u t g", b=2, u=4)[:, :, :, s, :]
                last = copy(dst, src)
            last.then_inc(done, 1)

        @block.scalar
        def _(act):
            def copy(dst, src):
                return act.activation(dst, src, ACT.Copy)

            def copy_selected(k, i):
                if i == 0:
                    at_least(act, products_made, TILES * GROUPS * k)
                act.wait_ge(one_hot_used, HALVES * k + 2 * i + 2)
                copy(feats[:, :, NG + i], ps_s[:, i % 2, 0:CHUNK]).then_inc(selected_copied, 1)

            def copy_turned(k, j, i):
                if i == 0:
                    at_least(act, products_made, TILES * GROUPS * (k - 1) + GROUPS * (j + 1))
                act.wait_ge(turned, TILES * NT * k + NT * j + i + 1)
                first, n = TURNS[i]
                dst = feats[:, j * TILE:(j + 1) * TILE, first:first + n].rearrange("p s f -> p f s")
                copy(dst, ps_t[:, 0:n, :]).then_inc(turned_copied, 1)

            def relu1(m, half):
                if half == 0:
                    act.wait_ge(l2_made, 1 + m)
                act.wait_ge(l1_made, 2 * m + half + 1)
                for n in range(2):
                    out = 2 * half + n
                    act.activation(h1[:, out, :], ps_m[:, n, :], ACT.Relu,
                                   bias=b1_sb[:, out:out + 1]).then_inc(h1_made, 1)

            def turn_of_loop(k, dense):
                for i in range(N_SELECTED):
                    copy_selected(k, i)
                    if i < NT:
                        copy_turned(k, 0, i)
                for kind, i in SECOND_HALF:
                    if kind == "turn":
                        copy_turned(k, 1, i)
                    if kind == "product":
                        copy_blocks(act, copy, k, i, (0, 1), blocks_by_act)
                    if kind == "layer1" and dense:
                        relu1(k - 1, i)

            for i in range(N_SELECTED):
                act.wait_ge(raw_loaded[i % STAGES], 16 * (i // STAGES + 1))
                src = raw[0:RP, (i % STAGES) * max(BLOCKS) * DIM:][:, 0:BLOCKS[i] * DIM]
                copy(table_hi[:, BLOCK_AT[i]:BLOCK_AT[i] + BLOCKS[i], :].rearrange("p b d -> p (b d)"),
                     src).then_inc(hi_made, 1)
            act.wait_ge(lo_made, N_SELECTED)
            turn_of_loop(0, False)
            act.wait_ge(weights_loaded, 16 * (KC + 4))
            with act.Fori(1, CHUNKS) as k:
                turn_of_loop(k, True)
            relu1(CHUNKS - 1, 0)
            relu1(CHUNKS - 1, 1)

        @block.vector
        def _(dve):
            def make_one_hot(k, i, h):
                if i == 0 and h == 0:
                    dve.wait_ge(ids_rep_loaded, 16 * (k + 1))
                at_least(dve, one_hot_used, HALVES * k + 2 * i + h - SETS + 1)
                n = BLOCKS[i] // 2
                for b in range(n):
                    at = BLOCK_AT[i] + h * n + b
                    last = dve.tensor_scalar(one_hot[:, (2 * i + h) % SETS, b, :], ids_rep[0:RP, i, :],
                                             row_id[:, at:at + 1], None, ALU.is_equal)
                last.then_inc(one_hot_made, 1)

            def relu2(m):
                dve.wait_ge(l3_made, 1 + m)
                dve.wait_ge(l2_made, 1 + m + 1)
                for n in range(N2):
                    dve.tensor_scalar(h2[:, n, :], ps_m[:, n, :], b2_sb[:, n:n + 1], 0.0,
                                      ALU.add, ALU.max).then_inc(h2_made, 1)

            def finish(m):
                dve.wait_ge(l3_made, 1 + m + 1)
                dve.tensor_copy(y_sb[:, bass.ds(m * TILES, TILES)], ps_m[:, 0, 0:TILES]).then_inc(y_made, 1)

            def turn_of_loop(k, dense):
                for i in range(N_SELECTED):
                    for h in range(2):
                        make_one_hot(k, i, h)
                for kind, i in SECOND_HALF:
                    if kind == "product":
                        copy_blocks(dve, dve.tensor_copy, k, i, (2, 3), blocks_by_dve)
                    if kind == "layer2" and dense:
                        relu2(k - 1)
                    if kind == "layer3" and dense:
                        finish(k - 1)

            dve.sem_inc(y_made)
            dve.memset(feats[:, :, NF:SLOT], 0.0).then_inc(pads_zeroed, 1)
            for i in range(N_SELECTED):
                src = raw[0:RP, (i % STAGES) * max(BLOCKS) * DIM:][:, 0:BLOCKS[i] * DIM]
                rows = slice(BLOCK_AT[i], BLOCK_AT[i] + BLOCKS[i])
                dve.wait_ge(hi_made, i + 1)
                dve.tensor_tensor(table_lo[:, rows, :].rearrange("p b d -> p (b d)"), src,
                                  table_hi[:, rows, :].rearrange("p b d -> p (b d)").bitcast(F32),
                                  ALU.subtract).then_inc(lo_made, 1)
            dve.wait_ge(lo_made, N_SELECTED)
            dve.wait_ge(row_ids_made, N_SELECTED)
            turn_of_loop(0, False)
            dve.wait_ge(weights_loaded, 16 * (KC + 4))
            with dve.Fori(1, CHUNKS) as k:
                turn_of_loop(k, True)
            relu2(CHUNKS - 1)
            finish(CHUNKS - 1)


def kernel(**inputs):
    import concourse.bacc as bacc
    from concourse.bass_utils import run_bass_kernel_spmd

    def tril_row(f, g):
        a, b = max(ORDER[f], ORDER[g]), min(ORDER[f], ORDER[g])
        return a * (a - 1) // 2 + b

    x = {name: np.asarray(a) for name, a in inputs.items()}
    w1_rows = [tril_row(f, g) for f, g in packed_rows()] + list(range(PAIRS, CONTRACT))
    laid = {
        "ids_gathered": x["ids"][:, GATHERED].reshape(BATCH // P, P, NG).transpose(1, 0, 2).reshape(P, -1),
        "ids_selected": x["ids"][:, SELECTED].T,
        "dense_t": x["dense_ctx"].T,
        "w1": x["W_top1"][w1_rows],
        "b1": x["b_top1"].reshape(N1, P).T,
        "w2": x["W_top2"],
        "b2": x["b_top2"].reshape(N2, P).T,
        "w3": x["W_top3"].reshape(N2, P).T,
    }
    for f in range(NF):
        laid[f"tbl_{f}"] = x[f"tbl_{f}"]

    nc = bacc.Bacc("TRN2", target_bir_lowering=False, num_devices=1)
    arrays, ap = {}, {}
    for name, a in laid.items():
        arrays[f"{name}_dram"] = np.ascontiguousarray(a)
        ap[name] = nc.dram_tensor(f"{name}_dram", a.shape, mybir.dt.from_np(a.dtype), kind="ExternalInput").ap()
    y = nc.dram_tensor("y_dram", (P, BATCH // P), F32, kind="ExternalOutput").ap()
    dlrm_program(nc, ap["ids_gathered"], ap["ids_selected"], [ap[f"tbl_{f}"] for f in range(NF)],
                 ap["dense_t"], ap["w1"], ap["b1"], ap["w2"], ap["b2"], ap["w3"], y)
    done = run_bass_kernel_spmd(nc, [arrays], core_ids=[0])
    return done.results[0]["y_dram"].T.reshape(BATCH, 1)
```

```python
from contextlib import ExitStack

import numpy as np

import concourse.bass as bass
from concourse import mybir

F32 = mybir.dt.float32
F32R = mybir.dt.float32r
I32 = mybir.dt.int32
ALU = mybir.AluOpType
ACT = mybir.ActivationFunctionType

P = 128
BATCH = 2048
DIM = 128
NF = 27
ROWS = [125000, 12500, 1250, 1250, 12500, 12500, 12500, 1250, 1250, 12500, 1250, 1250, 1250, 12500,
        1000, 12500, 1250, 12500, 1000, 1250, 1000, 1250, 1000, 1000, 1250, 1250, 1000]
N_SELECTED = 7
SELECTED = sorted(sorted(range(NF), key=lambda f: ROWS[f])[:N_SELECTED], key=lambda f: ROWS[f])
GATHERED = [f for f in range(NF) if f not in SELECTED]
NG = len(GATHERED)
ORDER = GATHERED + SELECTED

TILE = 128
TILES = 2
CHUNK = TILE * TILES
CHUNKS = BATCH // CHUNK
RP = 125
BLOCKS = [ROWS[f] // RP for f in SELECTED]
BLOCK_AT = [sum(BLOCKS[:i]) for i in range(N_SELECTED)]
SET = 4
SETS = [(i, b, min(SET, n - b)) for i, n in enumerate(BLOCKS) for b in range(0, n, SET)]
NS = len(SETS)
SET_RING = 5 if NS % 5 == 0 else 3
AHEAD = min(4, SET_RING)
STAGES = 5

SLOT = 32
QUAD = 4
MS = SLOT * (QUAD - 1) + NF
GROUP = 32
GROUPS = TILE // GROUP
TURNS = [(s, min(4, NG - s)) for s in range(0, NG, 4)]
NT = len(TURNS)
PAIRS = NF * (NF - 1) // 2
DENSE = 16
H1, H2 = 512, 256
N1, N2 = H1 // P, H2 // P
CONTRACT = PAIRS + DENSE
KC = -(-CONTRACT // P)

FIRST_HALF = [step for step in [("select", 0), ("select", 1), ("turn", 0), ("select", 2), ("turn", 1), ("select", 3),
              ("turn", 2), ("select", 4), ("turn", 3), ("select", 5), ("turn", 4), ("select", 6), ("select", 7), ("select", 8)]
              if step[0] == "turn" or step[1] < N_SELECTED]
SECOND_HALF = [("layer2", 2), ("turn", 0), ("product", 0), ("layer3", 2), ("product", 1), ("turn", 1),
               ("product", 2), ("turn", 2), ("layer1", 0), ("turn", 3), ("product", 3), ("turn", 4), ("layer1", 1),
               ("product", 4), ("product", 5), ("product", 6), ("product", 7)]
LAST_HALF = [("layer2", 2), ("product", 0), ("layer3", 2), ("product", 1), ("turn", 0), ("product", 2),
             ("turn", 1), ("layer1", 0), ("turn", 2), ("product", 3), ("layer1", 1), ("turn", 3), ("layer2", 1),
             ("turn", 4), ("product", 4), ("layer3", 1), ("product", 5), ("product", 6), ("product", 7)]

assert NT <= 5 and NS % SET_RING == 0 and all(ROWS[f] % RP == 0 for f in SELECTED)


def packing():
    runs, left = [], list(range(NF - 1))
    for c in range(KC):
        room = P if c < KC - 1 else PAIRS - (KC - 1) * P
        for g in list(left):
            if NF - 1 - g <= room:
                runs.append((g, NF - 1 - g, c, (P if c < KC - 1 else PAIRS - (KC - 1) * P) - room))
                room -= NF - 1 - g
                left.remove(g)
        assert room == 0
    assert not left
    return runs


RUNS = packing()
POOL_RUNS = [run for n, run in enumerate(RUNS) if n % 8 in (1, 4, 7)]
SYNC_RUNS = [run for run in RUNS if run not in POOL_RUNS]
REPACK = 16 * (len(RUNS) + 1)


def second_half(k):
    if not isinstance(k, int):
        return SECOND_HALF
    back = {"layer1": lambda i: 1, "layer2": lambda i: i, "layer3": lambda i: i}
    steps = LAST_HALF if k == CHUNKS - 1 else SECOND_HALF
    return [(kind, i) for kind, i in steps if kind not in back or back[kind](i) <= k]


def dlrm_program(nc, ids_gathered, ids_selected, tables, dense_t, w1, b1, w2, b2, w3, y):
    with ExitStack() as ctx:
        def sb(name, shape, dt=F32):
            return ctx.enter_context(nc.sbuf_tensor(name, shape, dt))

        def ps(name, shape):
            return ctx.enter_context(nc.psum_tensor(name, shape, F32))

        def sem(name):
            return ctx.enter_context(nc.semaphore(name))

        ids_all = sb("ids_all", [P, BATCH // P * NG], I32)
        ids_now = sb("ids_now", [P, TILES, NG], I32)
        gathered = sb("gathered", [P, TILES, NG, DIM])
        ids_rep = sb("ids_rep", [P, N_SELECTED, CHUNK], I32)
        table_hi = sb("table_hi", [RP, sum(BLOCKS), DIM], F32R)
        table_lo = sb("table_lo", [RP, sum(BLOCKS), DIM], F32R)
        row_id = sb("row_id", [RP, sum(BLOCKS)])
        one_hot = sb("one_hot", [RP, SET_RING, SET, CHUNK], F32R)
        feats = sb("feats", [P, CHUNK, SLOT])
        blocks = sb("blocks", [P, NF - 1, CHUNK])
        raw = blocks[:].rearrange("p g s -> p (g s)")
        packed = sb("packed", [P, KC, CHUNK])
        packed_last = sb("packed_last", [P, KC, CHUNK])
        w1_sb = sb("w1_sb", [P, KC, H1])
        w2_sb = sb("w2_sb", [P, N1, H2])
        w3_sb = sb("w3_sb", [P, N2])
        b1_sb = sb("b1_sb", [P, N1])
        b2_sb = sb("b2_sb", [P, N2])
        h1 = sb("h1", [P, N1, CHUNK])
        h2 = sb("h2", [P, N2, CHUNK])
        y_sb = sb("y_sb", [P, BATCH // TILE])
        ident = sb("ident", [P, P])

        ps_t = ps("ps_t", [P, 4, TILE])
        ps_s = ps("ps_s", [P, 2, 512])
        ps_g = ps("ps_g", [P, 2, 2, 512])
        ps_m = ps("ps_m", [P, 2, CHUNK])

        ps_last1 = [ps_m[:].rearrange("p a (b s) -> p (a b) s", s=TILE), ps_t[:]]
        ps_last2 = [ps_s[:, j, 0:N2 * TILE].rearrange("p (n s) -> p n s", s=TILE) for j in range(TILES)]

        ids_loaded = sem("ids_loaded")
        ids_staged = sem("ids_staged")
        gathers_begun = sem("gathers_begun")
        rows_gathered = [[sem(f"rows_gathered{j}_{i}") for i in range(NT)] for j in range(TILES)]
        ids_rep_loaded = sem("ids_rep_loaded")
        raw_loaded = [sem(f"raw_loaded{i}") for i in range(STAGES)]
        weights_loaded = sem("weights_loaded")
        hi_made = sem("hi_made")
        lo_made = sem("lo_made")
        row_ids_made = sem("row_ids_made")
        ident_zeroed = sem("ident_zeroed")
        ident_made = sem("ident_made")
        pads_zeroed = sem("pads_zeroed")
        one_hot_made = sem("one_hot_made")
        one_hot_used = sem("one_hot_used")
        selected_copied = sem("selected_copied")
        turned = sem("turned")
        turned_copied = sem("turned_copied")
        products_made = sem("products_made")
        blocks_by_act = sem("blocks_by_act")
        blocks_by_dve = sem("blocks_by_dve")
        packed_ready = sem("packed_ready")
        last_by_sync = [sem(f"last_by_sync{j}") for j in range(TILES)]
        last_by_pool = [sem(f"last_by_pool{j}") for j in range(TILES)]
        l1_made = sem("l1_made")
        h1_made = sem("h1_made")
        l2_made = sem("l2_made")
        h2_made = sem("h2_made")
        l3_made = sem("l3_made")
        y_made = sem("y_made")
        y_stored = sem("y_stored")

        def at_least(eng, semaphore, value):
            if not isinstance(value, int) or value > 0:
                eng.wait_ge(semaphore, value)

        block = ctx.enter_context(nc.Block())

        @block.sync
        def _(sp):
            def load_ids_rep(k):
                src = ids_selected[:, bass.ds(k * CHUNK, CHUNK)]
                sp.dma_start(ids_rep[:], src.partition_broadcast(P)).then_inc(ids_rep_loaded, 16)

            def pack(k):
                at_least(sp, l1_made, 2 * k)
                sp.dma_start(packed[PAIRS % P:PAIRS % P + DENSE, KC - 1, :],
                             dense_t[:, bass.ds(k * CHUNK, CHUNK)]).then_inc(packed_ready, 16)
                sp.wait_ge(blocks_by_act, TILES * GROUPS * (k + 1))
                sp.wait_ge(blocks_by_dve, TILES * GROUPS * (k + 1))
                for g, n, c, p in RUNS:
                    sp.dma_start(packed[p:p + n, c, :], blocks[g + 1:NF, g, :]).then_inc(packed_ready, 16)

            sp.dma_start(ids_all[:], ids_gathered).then_inc(ids_loaded, 16)
            load_ids_rep(0)
            for i, f in enumerate(SELECTED):
                if i >= STAGES:
                    sp.wait_ge(lo_made, i - STAGES + 1)
                sp.dma_start(raw[0:RP, (i % STAGES) * max(BLOCKS) * DIM:][:, 0:BLOCKS[i] * DIM],
                             tables[f].rearrange("(p b) d -> p (b d)", p=RP)).then_inc(raw_loaded[i % STAGES], 16)
            for c in range(KC):
                n = min(P, CONTRACT - c * P)
                sp.dma_start(w1_sb[0:n, c, :], w1[c * P:c * P + n, :]).then_inc(weights_loaded, 16)
            sp.dma_start(w2_sb[:], w2.rearrange("(c p) n -> p c n", p=P)).then_inc(weights_loaded, 16)
            sp.dma_start(w3_sb[:], w3).then_inc(weights_loaded, 16)
            sp.dma_start(b1_sb[:], b1).then_inc(weights_loaded, 16)
            sp.dma_start(b2_sb[:], b2).then_inc(weights_loaded, 16)

            sp.wait_ge(one_hot_made, NS)
            load_ids_rep(1)
            pack(0)
            with sp.Fori(1, CHUNKS - 1) as k:
                sp.wait_ge(one_hot_made, NS * (k + 1))
                load_ids_rep(k + 1)
                pack(k)
            last = CHUNKS - 1
            for j in range(TILES):
                cols = slice(j * TILE, (j + 1) * TILE)
                sp.dma_start(packed_last[PAIRS % P:PAIRS % P + DENSE, KC - 1, cols],
                             dense_t[:, last * CHUNK + j * TILE:][:, 0:TILE]).then_inc(last_by_sync[j], 16)
                sp.wait_ge(blocks_by_act, TILES * GROUPS * last + GROUPS * (j + 1))
                sp.wait_ge(blocks_by_dve, TILES * GROUPS * last + GROUPS * (j + 1))
                for g, n, c, p in SYNC_RUNS:
                    sp.dma_start(packed_last[p:p + n, c, cols], blocks[g + 1:NF, g, cols]
                                 ).then_inc(last_by_sync[j], 16)
            sp.wait_ge(y_made, 1 + CHUNKS - 1 + TILES)
            sp.dma_start(y, y_sb[:]).then_inc(y_stored, 16)
            sp.wait_ge(y_stored, 16)

        @block.gpsimd
        def _(pool):
            pool.memset(ident[:], 0.0).then_inc(ident_zeroed, 1)
            pool.wait_ge(ident_zeroed, 1)
            pool.affine_select(out=ident[:], in_=ident[:], compare_op=ALU.not_equal, fill=1.0, base=0,
                               pattern=[[-1, P]], channel_multiplier=1).then_inc(ident_made, 1)
            for at, n in zip(BLOCK_AT, BLOCKS):
                pool.iota(row_id[:, at:at + n], [[1, n]], base=0, channel_multiplier=n,
                          allow_small_or_imprecise_dtypes=True).then_inc(row_ids_made, 1)
            def gather(k):
                for j in range(TILES):
                    for i, (first, n) in enumerate(TURNS):
                        pool.wait_ge(ids_staged, TILES * NT * k + NT * j + i + 1)
                        pool.sem_inc(gathers_begun)
                        for s in range(first, first + n):
                            pool.indirect_dma_start(
                                gathered[:, j, s, :], None, tables[GATHERED[s]],
                                bass.IndirectOffsetOnAxis(ids_now[:, j, s:s + 1], 0),
                            ).then_inc(rows_gathered[j][i], 16)

            gather(0)
            with pool.Fori(1, CHUNKS) as k:
                gather(k)
            for j in range(TILES):
                cols = slice(j * TILE, (j + 1) * TILE)
                pool.wait_ge(blocks_by_act, TILES * GROUPS * (CHUNKS - 1) + GROUPS * (j + 1))
                pool.wait_ge(blocks_by_dve, TILES * GROUPS * (CHUNKS - 1) + GROUPS * (j + 1))
                for g, n, c, p in POOL_RUNS:
                    pool.dma_start(packed_last[p:p + n, c, cols], blocks[g + 1:NF, g, cols]
                                   ).then_inc(last_by_pool[j], 16)

        @block.tensor
        def _(pe):
            def select(k, i):
                if i == 0:
                    at_least(pe, selected_copied, N_SELECTED * k)
                elif i >= 2:
                    pe.wait_ge(selected_copied, N_SELECTED * k + i - 1)
                if isinstance(k, int):
                    pe.wait_ge(lo_made, i + 1)
                for at, (table, first, n) in enumerate(SETS):
                    if table != i:
                        continue
                    pe.wait_ge(one_hot_made, NS * k + at + 1)
                    for b in range(n):
                        rows, picks = BLOCK_AT[i] + first + b, one_hot[:, at % SET_RING, b, :]
                        pe.matmul(ps_s[:, i % 2, 0:CHUNK], table_hi[:, rows, :], picks, start=(first + b == 0),
                                  stop=False)
                        mm = pe.matmul(ps_s[:, i % 2, 0:CHUNK], table_lo[:, rows, :], picks, start=False,
                                       stop=(first + b == BLOCKS[i] - 1))
                    mm.then_inc(one_hot_used, 1)

            def turn(k, j, i):
                first, n = TURNS[i]
                pe.wait_ge(rows_gathered[j][i], 16 * n * (k + 1))
                at_least(pe, turned_copied, TILES * NT * k + NT * j + i)
                for s in range(n):
                    mm = pe.transpose(ps_t[:, s, :], gathered[:, j, first + s, :], ident[:])
                mm.then_inc(turned, 1)

            def product(k, j, q):
                if q == 0:
                    pe.wait_ge(turned_copied, TILES * NT * k + NT * (j + 1))
                if q == 0 and j == 0:
                    pe.wait_ge(selected_copied, N_SELECTED * (k + 1))
                n = GROUPS * j + q
                at_least(pe, blocks_by_act, TILES * GROUPS * k + n - 1)
                at_least(pe, blocks_by_dve, TILES * GROUPS * k + n - 1)
                for u in range(GROUP // QUAD):
                    s0 = j * TILE + q * GROUP + u * QUAD
                    four = feats[:, s0:s0 + QUAD, :]
                    out = ps_g[0:MS, n % 2, u // 4, (u % 4) * QUAD * (NF - 1):(u % 4 + 1) * QUAD * (NF - 1)]
                    mm = pe.matmul(out, four.rearrange("p s f -> p (s f)")[:, 0:MS], four[:, :, 0:NF - 1],
                                   start=True, stop=True)
                mm.then_inc(products_made, 1)

            def layer1(m, half):
                if half == 0:
                    pe.wait_ge(packed_ready, REPACK * (m + 1))
                    pe.wait_ge(y_made, 1 + m)
                else:
                    pe.wait_ge(h1_made, N1 * m + N1 // 2)
                for n in range(2):
                    out = 2 * half + n
                    for c in range(KC):
                        kk = min(P, CONTRACT - c * P)
                        mm = pe.matmul(ps_m[:, n, :], w1_sb[0:kk, c, out * P:(out + 1) * P],
                                       packed[0:kk, c, :], start=(c == 0), stop=(c == KC - 1))
                mm.then_inc(l1_made, 1)

            def layer2(m):
                pe.wait_ge(h1_made, N1 * (m + 1))
                for n in range(N2):
                    for c in range(N1):
                        mm = pe.matmul(ps_m[:, n, :], w2_sb[:, c, n * P:(n + 1) * P], h1[:, c, :],
                                       start=(c == 0), stop=(c == N1 - 1))
                mm.then_inc(l2_made, 1)

            def layer3(m):
                pe.wait_ge(h2_made, N2 * (m + 1))
                for j in range(TILES):
                    for c in range(N2):
                        mm = pe.matmul(ps_m[:, 0, j:j + 1], h2[:, c, j * TILE:(j + 1) * TILE],
                                       w3_sb[:, c:c + 1], start=(c == 0), stop=(c == N2 - 1))
                mm.then_inc(l3_made, 1)

            def turn_of_loop(k):
                for kind, i in FIRST_HALF:
                    if kind == "select":
                        select(k, i)
                    else:
                        turn(k, 0, i)
                for kind, i in second_half(k):
                    if kind == "turn":
                        turn(k, 1, i)
                    if kind == "product":
                        product(k, i // GROUPS, i % GROUPS)
                    if kind == "layer1":
                        layer1(k - 1, i)
                    if kind == "layer2":
                        layer2(k - i)
                    if kind == "layer3":
                        layer3(k - i)

            pe.sem_inc(l2_made)
            pe.sem_inc(l3_made)
            pe.wait_ge(ident_made, 1)
            pe.wait_ge(pads_zeroed, 1)
            turn_of_loop(0)
            pe.wait_ge(weights_loaded, 16 * (KC + 4))
            turn_of_loop(1)
            with pe.Fori(2, CHUNKS - 1) as k:
                turn_of_loop(k)
            turn_of_loop(CHUNKS - 1)
            m = CHUNKS - 1
            for j in range(TILES):
                if j == 0:
                    pe.wait_ge(y_made, 1 + m)
                    pe.wait_ge(selected_copied, N_SELECTED * CHUNKS)
                else:
                    pe.wait_ge(turned_copied, TILES * NT * CHUNKS)
                pe.wait_ge(last_by_sync[j], 16 * (len(SYNC_RUNS) + 1))
                pe.wait_ge(last_by_pool[j], 16 * len(POOL_RUNS))
                for n in range(N1):
                    for c in range(KC):
                        kk = min(P, CONTRACT - c * P)
                        mm = pe.matmul(ps_last1[j][:, n, :], w1_sb[0:kk, c, n * P:(n + 1) * P],
                                       packed_last[0:kk, c, j * TILE:(j + 1) * TILE],
                                       start=(c == 0), stop=(c == KC - 1))
                mm.then_inc(l1_made, 1)
                pe.wait_ge(h1_made, N1 * (m + j + 1))
                for n in range(N2):
                    for c in range(N1):
                        mm = pe.matmul(ps_last2[j][:, n, :], w2_sb[:, c, n * P:(n + 1) * P],
                                       h1[:, c, j * TILE:(j + 1) * TILE], start=(c == 0), stop=(c == N1 - 1))
                mm.then_inc(l2_made, 1)
                pe.wait_ge(h2_made, N2 * (m + j + 1))
                for c in range(N2):
                    mm = pe.matmul(ps_last1[j][:, 0, 0:1], h2[:, c, j * TILE:(j + 1) * TILE], w3_sb[:, c:c + 1],
                                   start=(c == 0), stop=(c == N2 - 1))
                mm.then_inc(l3_made, 1)

        def copy_blocks(eng, copy, k, n, samples, done):
            if n == 0:
                at_least(eng, packed_ready, REPACK * k)
            eng.wait_ge(products_made, TILES * GROUPS * k + n + 1)
            for s in samples:
                wide = ps_g[SLOT * s:SLOT * s + NF, n % 2, :, 0:4 * QUAD * (NF - 1)]
                src = wide.rearrange("p b (u t g) -> p b u t g", u=4, t=QUAD)[:, :, :, s, :]
                dst = blocks[0:NF, :, n * GROUP:(n + 1) * GROUP].rearrange(
                    "p g (b u t) -> p b u t g", b=2, u=4)[:, :, :, s, :]
                last = copy(dst, src)
            last.then_inc(done, 1)

        @block.scalar
        def _(act):
            def copy(dst, src):
                return act.activation(dst, src, ACT.Copy)

            def copy_selected(k, i):
                if i == 0:
                    at_least(act, products_made, TILES * GROUPS * k)
                act.wait_ge(one_hot_used, NS * k + sum(t <= i for t, _, _ in SETS))
                copy(feats[:, :, NG + i], ps_s[:, i % 2, 0:CHUNK]).then_inc(selected_copied, 1)

            def copy_turned(k, j, i, more):
                if i == 0:
                    at_least(act, products_made, TILES * GROUPS * (k - 1) + GROUPS * (j + 1))
                act.wait_ge(turned, TILES * NT * k + NT * j + i + 1)
                first, n = TURNS[i]
                dst = feats[:, j * TILE:(j + 1) * TILE, first:first + n].rearrange("p s f -> p f s")
                copy(dst, ps_t[:, 0:n, :]).then_inc(turned_copied, 1)
                if more:
                    stage_ids(k + 1, j, i)

            def stage_ids(k, j, i):
                first, n = TURNS[i]
                act.activation(ids_now[:, j, first:first + n],
                               ids_all[:, bass.ds((k * TILES + j) * NG + first, n)],
                               ACT.Copy).then_inc(ids_staged, 1)

            def relu1(m, half):
                if half == 0:
                    act.wait_ge(l2_made, 1 + m)
                act.wait_ge(l1_made, 2 * m + half + 1)
                for n in range(2):
                    out = 2 * half + n
                    act.activation(h1[:, out, :], ps_m[:, n, :], ACT.Relu,
                                   bias=b1_sb[:, out:out + 1]).then_inc(h1_made, 1)

            def turn_of_loop(k, more):
                for kind, i in FIRST_HALF:
                    if kind == "select":
                        copy_selected(k, i)
                    else:
                        copy_turned(k, 0, i, more)
                if isinstance(k, int) and k == 0:
                    act.wait_ge(lo_made, N_SELECTED)
                for kind, i in second_half(k):
                    if kind == "turn":
                        copy_turned(k, 1, i, more)
                    if kind == "product":
                        copy_blocks(act, copy, k, i, (0, 1), blocks_by_act)
                    if kind == "layer1":
                        relu1(k - 1, i)

            act.wait_ge(ids_loaded, 16)
            for j in range(TILES):
                for i in range(NT):
                    stage_ids(0, j, i)
            for i in range(N_SELECTED):
                act.wait_ge(raw_loaded[i % STAGES], 16 * (i // STAGES + 1))
                src = raw[0:RP, (i % STAGES) * max(BLOCKS) * DIM:][:, 0:BLOCKS[i] * DIM]
                copy(table_hi[:, BLOCK_AT[i]:BLOCK_AT[i] + BLOCKS[i], :].rearrange("p b d -> p (b d)"),
                     src).then_inc(hi_made, 1)
            turn_of_loop(0, True)
            act.wait_ge(weights_loaded, 16 * (KC + 4))
            turn_of_loop(1, True)
            with act.Fori(2, CHUNKS - 1) as k:
                turn_of_loop(k, True)
            turn_of_loop(CHUNKS - 1, False)
            m = CHUNKS - 1
            act.wait_ge(l2_made, 1 + m)
            for j in range(TILES):
                act.wait_ge(l1_made, 2 * m + j + 1)
                for n in range(N1):
                    act.activation(h1[:, n, j * TILE:(j + 1) * TILE], ps_last1[j][:, n, :], ACT.Relu,
                                   bias=b1_sb[:, n:n + 1]).then_inc(h1_made, 1)

        @block.vector
        def _(dve):
            def make_one_hot(k, at):
                i, first, n = SETS[at]
                if at == 0:
                    dve.wait_ge(ids_rep_loaded, 16 * (k + 1))
                at_least(dve, one_hot_used, NS * k + at - SET_RING + 1)
                for b in range(n):
                    rows = BLOCK_AT[i] + first + b
                    last = dve.tensor_scalar(one_hot[:, at % SET_RING, b, :], ids_rep[0:RP, i, :],
                                             row_id[:, rows:rows + 1], None, ALU.is_equal)
                last.then_inc(one_hot_made, 1)

            def relu2(m):
                dve.wait_ge(l3_made, 1 + m)
                dve.wait_ge(l2_made, 1 + m + 1)
                for n in range(N2):
                    dve.tensor_scalar(h2[:, n, :], ps_m[:, n, :], b2_sb[:, n:n + 1], 0.0,
                                      ALU.add, ALU.max).then_inc(h2_made, 1)

            def finish(m):
                dve.wait_ge(l3_made, 1 + m + 1)
                dve.tensor_copy(y_sb[:, bass.ds(m * TILES, TILES)], ps_m[:, 0, 0:TILES]).then_inc(y_made, 1)

            def turn_of_loop(k, more):
                for at in range(AHEAD, NS):
                    make_one_hot(k, at)
                for kind, i in second_half(k):
                    if kind == "product":
                        copy_blocks(dve, dve.tensor_copy, k, i, (2, 3), blocks_by_dve)
                        ahead = i - (TILES * GROUPS - AHEAD)
                        if more and ahead >= 0:
                            make_one_hot(k + 1, ahead)
                    if kind == "layer2":
                        relu2(k - i)
                    if kind == "layer3":
                        finish(k - i)

            dve.sem_inc(y_made)
            dve.memset(feats[:, :, NF:SLOT], 0.0).then_inc(pads_zeroed, 1)
            dve.wait_ge(row_ids_made, N_SELECTED)
            for i in range(N_SELECTED):
                src = raw[0:RP, (i % STAGES) * max(BLOCKS) * DIM:][:, 0:BLOCKS[i] * DIM]
                rows = slice(BLOCK_AT[i], BLOCK_AT[i] + BLOCKS[i])
                dve.wait_ge(hi_made, i + 1)
                dve.tensor_tensor(table_lo[:, rows, :].rearrange("p b d -> p (b d)"), src,
                                  table_hi[:, rows, :].rearrange("p b d -> p (b d)").bitcast(F32),
                                  ALU.subtract).then_inc(lo_made, 1)
                for at in range(AHEAD):
                    if SETS[at][0] == i:
                        make_one_hot(0, at)
            dve.wait_ge(lo_made, N_SELECTED)
            turn_of_loop(0, True)
            dve.wait_ge(weights_loaded, 16 * (KC + 4))
            turn_of_loop(1, True)
            with dve.Fori(2, CHUNKS - 1) as k:
                turn_of_loop(k, True)
            turn_of_loop(CHUNKS - 1, False)
            m = CHUNKS - 1
            dve.wait_ge(l3_made, 1 + m)
            for j in range(TILES):
                dve.wait_ge(l2_made, 1 + m + j + 1)
                for n in range(N2):
                    dve.tensor_scalar(h2[:, n, j * TILE:(j + 1) * TILE], ps_last2[j][:, n, :],
                                      b2_sb[:, n:n + 1], 0.0, ALU.add, ALU.max).then_inc(h2_made, 1)
                dve.wait_ge(l3_made, 1 + m + j + 1)
                dve.tensor_copy(y_sb[:, m * TILES + j:m * TILES + j + 1],
                                ps_last1[j][:, 0, 0:1]).then_inc(y_made, 1)


def kernel(**inputs):
    import concourse.bacc as bacc
    from concourse.bass_utils import run_bass_kernel_spmd

    def tril_row(f, g):
        a, b = max(ORDER[f], ORDER[g]), min(ORDER[f], ORDER[g])
        return a * (a - 1) // 2 + b

    x = {name: np.asarray(a) for name, a in inputs.items()}
    w1_rows = [tril_row(f, g) for g, _, _, _ in RUNS for f in range(g + 1, NF)] + list(range(PAIRS, CONTRACT))
    laid = {
        "ids_gathered": x["ids"][:, GATHERED].reshape(BATCH // P, P, NG).transpose(1, 0, 2).reshape(P, -1),
        "ids_selected": x["ids"][:, SELECTED].T,
        "dense_t": x["dense_ctx"].T,
        "w1": x["W_top1"][w1_rows],
        "b1": x["b_top1"].reshape(N1, P).T,
        "w2": x["W_top2"],
        "b2": x["b_top2"].reshape(N2, P).T,
        "w3": x["W_top3"].reshape(N2, P).T,
    }
    for f in range(NF):
        laid[f"tbl_{f}"] = x[f"tbl_{f}"]

    nc = bacc.Bacc("TRN2", target_bir_lowering=False, num_devices=1)
    arrays, ap = {}, {}
    for name, a in laid.items():
        arrays[f"{name}_dram"] = np.ascontiguousarray(a)
        ap[name] = nc.dram_tensor(f"{name}_dram", a.shape, mybir.dt.from_np(a.dtype), kind="ExternalInput").ap()
    y = nc.dram_tensor("y_dram", (P, BATCH // P), F32, kind="ExternalOutput").ap()
    dlrm_program(nc, ap["ids_gathered"], ap["ids_selected"], [ap[f"tbl_{f}"] for f in range(NF)],
                 ap["dense_t"], ap["w1"], ap["b1"], ap["w2"], ap["b2"], ap["w3"], y)
    done = run_bass_kernel_spmd(nc, [arrays], core_ids=[0])
    return done.results[0]["y_dram"].T.reshape(BATCH, 1)
```

```python
from contextlib import ExitStack

import numpy as np

import concourse.bass as bass
from concourse import mybir

F32 = mybir.dt.float32
F32R = mybir.dt.float32r
I32 = mybir.dt.int32
ALU = mybir.AluOpType
ACT = mybir.ActivationFunctionType

P = 128
BATCH = 2048
DIM = 128
NF = 27
ROWS = [125000, 12500, 1250, 1250, 12500, 12500, 12500, 1250, 1250, 12500, 1250, 1250, 1250, 12500,
        1000, 12500, 1250, 12500, 1000, 1250, 1000, 1250, 1000, 1000, 1250, 1250, 1000]
N_SELECTED = 8
SELECTED = sorted(range(NF), key=lambda f: ROWS[f])[:N_SELECTED]
SHARED = SELECTED[-1]
GATHERED = [f for f in range(NF) if f not in SELECTED] + [SHARED]
NG = len(GATHERED)
ORDER = GATHERED + SELECTED[:-1]

TILE = 128
TILES = 2
CHUNK = TILE * TILES
CHUNKS = BATCH // CHUNK
RP = 125
BLOCKS = [ROWS[f] // RP for f in SELECTED]
BLOCK_AT = [sum(BLOCKS[:i]) for i in range(N_SELECTED)]
WIDTH = [CHUNK] * (N_SELECTED - 1) + [TILE]
SELECTED_SLOT = [NG + i for i in range(N_SELECTED - 1)] + [NG - 1]
SET = 5
SETS = [(i, b, min(SET * CHUNK // WIDTH[i], n - b)) for i, n in enumerate(BLOCKS)
        for b in range(0, n, SET * CHUNK // WIDTH[i])]
NS = len(SETS)
SETS_SHARED = sum(i == N_SELECTED - 1 for i, _, _ in SETS)
SET_RING = 5
AHEAD = SET_RING
IDS_PIECE = 2
RAW_AHEAD = 4
RAW_IN_GATHERED = 2

SLOT = 32
QUAD = 4
MS = SLOT * (QUAD - 1) + NF
GROUP = 32
GROUPS = TILE // GROUP
NT = -(-NG // 4)
PAIRS = NF * (NF - 1) // 2
PACKED = PAIRS + NF // 2
DENSE = 16
H1, H2 = 512, 256
N1, N2 = H1 // P, H2 // P
CONTRACT = PACKED + DENSE
KC = -(-CONTRACT // P)
DENSE_AT = PACKED % P


def is_first(k):
    return isinstance(k, int) and k == 0


def is_last(k):
    return isinstance(k, int) and k == CHUNKS - 1


def turns(k, j):
    slots = NG - 1 if j == 1 and not is_last(k) else NG
    return [(s, min(4, slots - s)) for s in range(0, NG, 4)]


PRODUCTS_1 = [("product", 4), ("product", 5), ("product", 6), ("product", 7)]
STEPS_0 = [("select", 0), ("select", 1), ("select", 2), ("turn0", 0), ("select", 3), ("turn0", 1), ("turn0", 2),
           ("select", 4), ("turn0", 3), ("select", 5), ("turn0", 4), ("select", 6), ("turn1", 0), ("product", 0),
           ("product", 1), ("select", 7), ("turn1", 1), ("product", 2), ("turn1", 2), ("product", 3), ("turn1", 3),
           ("turn1", 4)] + PRODUCTS_1
STEPS_1 = [("select", 0), ("select", 1), ("turn0", 0), ("select", 2), ("turn0", 1), ("select", 3), ("turn0", 2),
           ("select", 4), ("turn0", 3), ("select", 5), ("select", 6), ("layer1", 0), ("turn0", 4), ("select", 7),
           ("turn1", 0), ("product", 0), ("product", 1), ("turn1", 1), ("product", 2), ("turn1", 2), ("product", 3),
           ("turn1", 3), ("layer1", 1), ("turn1", 4)] + PRODUCTS_1
STEPS = [("select", 0), ("select", 1), ("turn0", 0), ("select", 2), ("turn0", 1), ("select", 3), ("turn0", 2),
         ("select", 4), ("turn0", 3), ("select", 5), ("turn0", 4), ("select", 6), ("layer2", 2), ("turn1", 0),
         ("product", 0), ("layer3", 2), ("product", 1), ("select", 7), ("turn1", 1), ("product", 2), ("turn1", 2),
         ("layer1", 0), ("turn1", 3), ("product", 3), ("turn1", 4), ("layer1", 1)] + PRODUCTS_1
STEPS_LAST = [("select", 0), ("select", 1), ("turn0", 0), ("select", 2), ("turn0", 1), ("select", 3), ("turn0", 2),
              ("select", 4), ("turn0", 3), ("select", 5), ("turn0", 4), ("select", 6), ("layer2", 2), ("product", 0),
              ("layer3", 2), ("turn1", 0), ("product", 1), ("turn1", 1), ("product", 2), ("turn1", 2),
              ("layer1", 0), ("turn1", 3), ("product", 3), ("turn1", 4), ("layer1", 1)] + PRODUCTS_1 + [
              ("last1", 0), ("layer2", 1), ("last2", 0), ("layer3", 1), ("last3", 0), ("last1", 1), ("last2", 1),
              ("last3", 1)]

assert NT == 5 and N_SELECTED == 8 and TILES == 2 and GROUPS == 4
assert NS % SET_RING == 0 and all(ROWS[f] % RP == 0 for f in SELECTED)
assert N_SELECTED % IDS_PIECE == 0
assert (NG - 1) % 4 > 0
assert N1 + N2 <= N_SELECTED and N1 == 4


def packing():
    runs, left = [], list(range(0, NF - 1, 2))
    for c in range(KC):
        room = size = P if c < KC - 1 else DENSE_AT
        for g in list(left):
            if 2 * (NF - 1 - g) <= room:
                runs.append((g, NF - 1 - g, c, size - room))
                room -= 2 * (NF - 1 - g)
                left.remove(g)
    assert not left
    return runs


RUNS = packing()
POOL_RUNS = [run for n, run in enumerate(RUNS) if n % 8 in (1, 4, 7)]
SYNC_RUNS = [run for run in RUNS if run not in POOL_RUNS]
REPACK = 16 * (len(RUNS) + 1)


def steps(k):
    return {0: STEPS_0, 1: STEPS_1, CHUNKS - 1: STEPS_LAST}[k] if isinstance(k, int) else STEPS


def dlrm_program(nc, ids_gathered, ids_selected, tables, dense_t, w1, b1, w2, b2, w3, y):
    with ExitStack() as ctx:
        def sb(name, shape, dt=F32):
            return ctx.enter_context(nc.sbuf_tensor(name, shape, dt))

        def ps(name, shape):
            return ctx.enter_context(nc.psum_tensor(name, shape, F32))

        def sem(name):
            return ctx.enter_context(nc.semaphore(name))

        ids_all = sb("ids_all", [P, BATCH // P * NG], I32)
        ids_now = sb("ids_now", [P, TILES, NG], I32)
        gathered = sb("gathered", [P, TILES, NG, DIM])
        ids_rep = sb("ids_rep", [P, N_SELECTED, CHUNK], I32)
        table_hi = sb("table_hi", [RP, sum(BLOCKS), DIM], F32R)
        table_lo = sb("table_lo", [RP, sum(BLOCKS), DIM], F32R)
        row_id = sb("row_id", [RP, sum(BLOCKS)])
        one_hot = sb("one_hot", [RP, SET_RING, SET * CHUNK], F32R)
        feats = sb("feats", [P, CHUNK, SLOT])
        blocks = sb("blocks", [P, NF - 1, CHUNK])
        packed = sb("packed", [P, KC, CHUNK])
        packed_last = sb("packed_last", [P, KC, CHUNK])
        w1_sb = sb("w1_sb", [P, KC, H1])
        w2_sb = sb("w2_sb", [P, N1, H2])
        w3_sb = sb("w3_sb", [P, N2])
        b1_sb = sb("b1_sb", [P, N1])
        b2_sb = sb("b2_sb", [P, N2])
        h1 = sb("h1", [P, N1, CHUNK])
        h2 = sb("h2", [P, N2, CHUNK])
        y_sb = sb("y_sb", [P, BATCH // TILE])
        ident = sb("ident", [P, P])

        ps_t = ps("ps_t", [P, 4, TILE])
        ps_s = ps("ps_s", [P, 2, 512])
        ps_g = ps("ps_g", [P, 2, 2, 512])
        ps_m = ps("ps_m", [P, 2, CHUNK])

        ps_last1 = [[ps_t[:, n, :] for n in range(N1)], [ps_g[:, n // 2, n % 2, 0:TILE] for n in range(N1)]]
        ps_last2 = [[ps_s[:, j, n * TILE:(n + 1) * TILE] for n in range(N2)] for j in range(TILES)]
        h_last = ids_rep[:].bitcast(F32)

        ids_loaded = sem("ids_loaded")
        ids_staged = sem("ids_staged")
        gathers_begun = sem("gathers_begun")
        rows_gathered = [[sem(f"rows_gathered{j}_{i}") for i in range(NT)] for j in range(TILES)]
        ids_rep_loaded = sem("ids_rep_loaded")
        raw_loaded = [sem(f"raw_loaded{i}") for i in range(N_SELECTED)]
        weights_loaded = sem("weights_loaded")
        hi_made = sem("hi_made")
        lo_made = sem("lo_made")
        row_ids_made = sem("row_ids_made")
        ident_zeroed = sem("ident_zeroed")
        ident_made = sem("ident_made")
        pads_zeroed = sem("pads_zeroed")
        one_hot_made = sem("one_hot_made")
        one_hot_used = sem("one_hot_used")
        selected_copied = sem("selected_copied")
        turned = sem("turned")
        turned_copied = sem("turned_copied")
        products_made = sem("products_made")
        blocks_by_act = sem("blocks_by_act")
        blocks_by_dve = sem("blocks_by_dve")
        packed_ready = sem("packed_ready")
        last_by_sync = [[sem(f"last_by_sync{j}_{c}") for c in range(KC)] for j in range(TILES)]
        last_by_pool = [[sem(f"last_by_pool{j}_{c}") for c in range(KC)] for j in range(TILES)]
        l1_made = sem("l1_made")
        h1_made = sem("h1_made")
        l2_made = sem("l2_made")
        h2_made = sem("h2_made")
        l3_made = sem("l3_made")
        y_made = sem("y_made")
        y_stored = sem("y_stored")

        def raw_table(i):
            place, first = (gathered[:, 1], 0) if i < RAW_IN_GATHERED else (blocks[:], RAW_IN_GATHERED)
            at = (BLOCK_AT[i] - BLOCK_AT[first]) * DIM
            return place.rearrange("p a b -> p (a b)")[0:RP, at:at + BLOCKS[i] * DIM]

        def at_least(eng, semaphore, value):
            if not isinstance(value, int) or value > 0:
                eng.wait_ge(semaphore, value)

        def pack_run(to, run, cols):
            g, n, c, p = run
            return (to[p:p + 2 * n, c, cols], blocks[g + 1:NF, g:g + 2, cols])

        block = ctx.enter_context(nc.Block())

        @block.sync
        def _(sp):
            def load_ids_rep(k):
                for i in range(0, N_SELECTED, IDS_PIECE):
                    src = ids_selected[i:i + IDS_PIECE, bass.ds(k * CHUNK, CHUNK)]
                    sp.dma_start(ids_rep[:, i:i + IDS_PIECE, :], src.partition_broadcast(P)
                                 ).then_inc(ids_rep_loaded, 16)

            def pack(k):
                at_least(sp, l1_made, 2 * k)
                sp.dma_start(packed[DENSE_AT:DENSE_AT + DENSE, KC - 1, :],
                             dense_t[:, bass.ds(k * CHUNK, CHUNK)]).then_inc(packed_ready, 16)
                sp.wait_ge(blocks_by_act, TILES * GROUPS * (k + 1))
                sp.wait_ge(blocks_by_dve, TILES * GROUPS * (k + 1))
                for run in RUNS:
                    sp.dma_start(*pack_run(packed, run, slice(0, CHUNK))).then_inc(packed_ready, 16)

            sp.dma_start(ids_all[:], ids_gathered).then_inc(ids_loaded, 16)
            for i, f in enumerate(SELECTED):
                sp.dma_start(raw_table(i), tables[f].rearrange("(p b) d -> p (b d)", p=RP)).then_inc(raw_loaded[i], 16)
                if i == 0:
                    load_ids_rep(0)
            for c in range(KC):
                n = min(P, CONTRACT - c * P)
                sp.dma_start(w1_sb[0:n, c, :], w1[c * P:c * P + n, :]).then_inc(weights_loaded, 16)
            sp.dma_start(w2_sb[:], w2.rearrange("(c p) n -> p c n", p=P)).then_inc(weights_loaded, 16)
            sp.dma_start(w3_sb[:], w3).then_inc(weights_loaded, 16)
            sp.dma_start(b1_sb[:], b1).then_inc(weights_loaded, 16)
            sp.dma_start(b2_sb[:], b2).then_inc(weights_loaded, 16)

            sp.wait_ge(one_hot_made, NS)
            load_ids_rep(1)
            pack(0)
            with sp.Fori(1, CHUNKS - 1) as k:
                sp.wait_ge(one_hot_made, NS * (k + 1))
                load_ids_rep(k + 1)
                pack(k)
            last = CHUNKS - 1
            for j in range(TILES):
                cols = slice(j * TILE, (j + 1) * TILE)
                sp.dma_start(packed_last[DENSE_AT:DENSE_AT + DENSE, KC - 1, cols],
                             dense_t[:, last * CHUNK + j * TILE:][:, 0:TILE]).then_inc(last_by_sync[j][KC - 1], 16)
                sp.wait_ge(blocks_by_act, TILES * GROUPS * last + GROUPS * (j + 1))
                sp.wait_ge(blocks_by_dve, TILES * GROUPS * last + GROUPS * (j + 1))
                for run in SYNC_RUNS:
                    sp.dma_start(*pack_run(packed_last, run, cols)).then_inc(last_by_sync[j][run[2]], 16)
            sp.wait_ge(y_made, 1 + CHUNKS - 1 + TILES)
            sp.dma_start(y, y_sb[:]).then_inc(y_stored, 16)
            sp.wait_ge(y_stored, 16)

        @block.gpsimd
        def _(pool):
            pool.memset(ident[:], 0.0).then_inc(ident_zeroed, 1)
            pool.wait_ge(ident_zeroed, 1)
            pool.affine_select(out=ident[:], in_=ident[:], compare_op=ALU.not_equal, fill=1.0, base=0,
                               pattern=[[-1, P]], channel_multiplier=1).then_inc(ident_made, 1)
            for at, n in zip(BLOCK_AT, BLOCKS):
                pool.iota(row_id[:, at:at + n], [[1, n]], base=0, channel_multiplier=n,
                          allow_small_or_imprecise_dtypes=True).then_inc(row_ids_made, 1)

            def gather(k):
                for j in range(TILES):
                    if is_first(k) and j == 1:
                        pool.wait_ge(lo_made, RAW_IN_GATHERED)
                    for i, (first, n) in enumerate(turns(k, j)):
                        pool.wait_ge(ids_staged, TILES * NT * k + NT * j + i + 1)
                        pool.sem_inc(gathers_begun)
                        for s in range(first, first + n):
                            pool.indirect_dma_start(
                                gathered[:, j, s, :], None, tables[GATHERED[s]],
                                bass.IndirectOffsetOnAxis(ids_now[:, j, s:s + 1], 0),
                            ).then_inc(rows_gathered[j][i], 16)

            gather(0)
            with pool.Fori(1, CHUNKS - 1) as k:
                gather(k)
            gather(CHUNKS - 1)
            for j in range(TILES):
                cols = slice(j * TILE, (j + 1) * TILE)
                pool.wait_ge(blocks_by_act, TILES * GROUPS * (CHUNKS - 1) + GROUPS * (j + 1))
                pool.wait_ge(blocks_by_dve, TILES * GROUPS * (CHUNKS - 1) + GROUPS * (j + 1))
                for run in POOL_RUNS:
                    pool.dma_start(*pack_run(packed_last, run, cols)).then_inc(last_by_pool[j][run[2]], 16)

        @block.tensor
        def _(pe):
            def select(k, i):
                if i == 0:
                    at_least(pe, selected_copied, N_SELECTED * k)
                elif i >= 2:
                    pe.wait_ge(selected_copied, N_SELECTED * k + i - 1)
                if isinstance(k, int):
                    pe.wait_ge(lo_made, i + 1)
                width = WIDTH[i]
                for at, (table, first, n) in enumerate(SETS):
                    if table != i:
                        continue
                    pe.wait_ge(one_hot_made, NS * k + at + 1)
                    for b in range(n):
                        rows, picks = BLOCK_AT[i] + first + b, one_hot[:, at % SET_RING, b * width:(b + 1) * width]
                        pe.matmul(ps_s[:, i % 2, 0:width], table_hi[:, rows, :], picks, start=(first + b == 0),
                                  stop=False)
                        mm = pe.matmul(ps_s[:, i % 2, 0:width], table_lo[:, rows, :], picks, start=False,
                                       stop=(first + b == BLOCKS[i] - 1))
                    mm.then_inc(one_hot_used, 1)

            def turn(k, j, i):
                first, n = turns(k, j)[i]
                pe.wait_ge(rows_gathered[j][i], 16 * (n + k * turns(0, j)[i][1]))
                at_least(pe, turned_copied, TILES * NT * k + NT * j + i)
                for s in range(n):
                    mm = pe.transpose(ps_t[:, s, :], gathered[:, j, first + s, :], ident[:])
                mm.then_inc(turned, 1)

            def product(k, j, q):
                if q == 0:
                    pe.wait_ge(turned_copied, TILES * NT * k + NT * (j + 1))
                    pe.wait_ge(selected_copied, N_SELECTED * (k + 1) - (j == 0 or is_last(k)))
                n = GROUPS * j + q
                at_least(pe, blocks_by_act, TILES * GROUPS * k + n - 1)
                at_least(pe, blocks_by_dve, TILES * GROUPS * k + n - 1)
                for u in range(GROUP // QUAD):
                    s0 = j * TILE + q * GROUP + u * QUAD
                    four = feats[:, s0:s0 + QUAD, :]
                    out = ps_g[0:MS, n % 2, u // 4, (u % 4) * QUAD * (NF - 1):(u % 4 + 1) * QUAD * (NF - 1)]
                    mm = pe.matmul(out, four.rearrange("p s f -> p (s f)")[:, 0:MS], four[:, :, 0:NF - 1],
                                   start=True, stop=True)
                mm.then_inc(products_made, 1)

            def layer1(m, half):
                if half == 0:
                    pe.wait_ge(packed_ready, REPACK * (m + 1))
                    pe.wait_ge(y_made, 1 + m)
                else:
                    pe.wait_ge(h1_made, N1 * m + N1 // 2)
                for n in range(2):
                    out = 2 * half + n
                    for c in range(KC):
                        kk = min(P, CONTRACT - c * P)
                        mm = pe.matmul(ps_m[:, n, :], w1_sb[0:kk, c, out * P:(out + 1) * P],
                                       packed[0:kk, c, :], start=(c == 0), stop=(c == KC - 1))
                mm.then_inc(l1_made, 1)

            def layer2(m):
                pe.wait_ge(h1_made, N1 * (m + 1))
                for n in range(N2):
                    for c in range(N1):
                        mm = pe.matmul(ps_m[:, n, :], w2_sb[:, c, n * P:(n + 1) * P], h1[:, c, :],
                                       start=(c == 0), stop=(c == N1 - 1))
                mm.then_inc(l2_made, 1)

            def layer3(m):
                pe.wait_ge(h2_made, N2 * (m + 1))
                for j in range(TILES):
                    for c in range(N2):
                        mm = pe.matmul(ps_m[:, 0, j:j + 1], h2[:, c, j * TILE:(j + 1) * TILE],
                                       w3_sb[:, c:c + 1], start=(c == 0), stop=(c == N2 - 1))
                mm.then_inc(l3_made, 1)

            def last1(j):
                if j == 0:
                    pe.wait_ge(turned_copied, TILES * NT * CHUNKS)
                    steps = [(n, c) for n in range(N1) for c in range(KC)]
                else:
                    pe.wait_ge(blocks_by_act, TILES * GROUPS * CHUNKS)
                    pe.wait_ge(blocks_by_dve, TILES * GROUPS * CHUNKS)
                    steps = [(n, c) for c in range(KC) for n in range(N1)]
                for n, c in steps:
                    if n == 0:
                        by_sync = sum(run[2] == c for run in SYNC_RUNS) + (c == KC - 1)
                        pe.wait_ge(last_by_sync[j][c], 16 * by_sync)
                        pe.wait_ge(last_by_pool[j][c], 16 * sum(run[2] == c for run in POOL_RUNS))
                    kk = min(P, CONTRACT - c * P)
                    mm = pe.matmul(ps_last1[j][n], w1_sb[0:kk, c, n * P:(n + 1) * P],
                                   packed_last[0:kk, c, j * TILE:(j + 1) * TILE],
                                   start=(c == 0), stop=(c == KC - 1))
                    if c == KC - 1 and (j == 1 or n == N1 - 1):
                        mm.then_inc(l1_made, 1)

            def last2(j):
                if j == 0:
                    pe.wait_ge(selected_copied, N_SELECTED * CHUNKS - 1)
                for n in range(N2):
                    for c in range(N1):
                        if n == 0:
                            pe.wait_ge(h1_made, N1 * (CHUNKS - 1 + j) + c + 1)
                        mm = pe.matmul(ps_last2[j][n], w2_sb[:, c, n * P:(n + 1) * P],
                                       h_last[:, c, j * TILE:(j + 1) * TILE], start=(c == 0), stop=(c == N1 - 1))
                mm.then_inc(l2_made, 1)

            def last3(j):
                pe.wait_ge(h2_made, N2 * (CHUNKS + j))
                for c in range(N2):
                    mm = pe.matmul(ps_last1[j][0][:, 0:1], h_last[:, N1 + c, j * TILE:(j + 1) * TILE],
                                   w3_sb[:, c:c + 1], start=(c == 0), stop=(c == N2 - 1))
                mm.then_inc(l3_made, 1)

            def turn_of_loop(k):
                for kind, i in steps(k):
                    if kind == "select":
                        select(k, i)
                    if kind == "turn0":
                        turn(k, 0, i)
                    if kind == "turn1":
                        turn(k, 1, i)
                    if kind == "product":
                        product(k, i // GROUPS, i % GROUPS)
                    if kind == "layer1":
                        layer1(k - 1, i)
                    if kind == "layer2":
                        layer2(k - i)
                    if kind == "layer3":
                        layer3(k - i)
                    if kind == "last1":
                        last1(i)
                    if kind == "last2":
                        last2(i)
                    if kind == "last3":
                        last3(i)

            pe.sem_inc(l2_made)
            pe.sem_inc(l3_made)
            pe.wait_ge(ident_made, 1)
            pe.wait_ge(pads_zeroed, 1)
            turn_of_loop(0)
            pe.wait_ge(weights_loaded, 16 * (KC + 4))
            turn_of_loop(1)
            with pe.Fori(2, CHUNKS - 1) as k:
                turn_of_loop(k)
            turn_of_loop(CHUNKS - 1)

        def copy_blocks(eng, copy, k, n, samples, done):
            if n == 0:
                at_least(eng, packed_ready, REPACK * k)
            eng.wait_ge(products_made, TILES * GROUPS * k + n + 1)
            for s in samples:
                wide = ps_g[SLOT * s:SLOT * s + NF, n % 2, :, 0:4 * QUAD * (NF - 1)]
                src = wide.rearrange("p b (u t g) -> p b u t g", u=4, t=QUAD)[:, :, :, s, :]
                dst = blocks[0:NF, :, n * GROUP:(n + 1) * GROUP].rearrange(
                    "p g (b u t) -> p b u t g", b=2, u=4)[:, :, :, s, :]
                last = copy(dst, src)
            last.then_inc(done, 1)

        @block.scalar
        def _(act):
            def copy(dst, src):
                return act.activation(dst, src, ACT.Copy)

            def make_hi(i):
                act.wait_ge(raw_loaded[i], 16)
                copy(table_hi[:, BLOCK_AT[i]:BLOCK_AT[i] + BLOCKS[i], :].rearrange("p b d -> p (b d)"),
                     raw_table(i)).then_inc(hi_made, 1)

            def copy_selected(k, i):
                if i == 0:
                    at_least(act, products_made, TILES * GROUPS * k)
                act.wait_ge(one_hot_used, NS * k + sum(t <= i for t, _, _ in SETS))
                copy(feats[:, CHUNK - WIDTH[i]:, SELECTED_SLOT[i]], ps_s[:, i % 2, 0:WIDTH[i]]).then_inc(selected_copied, 1)

            def copy_turned(k, j, i, more):
                if i == 0:
                    at_least(act, products_made, TILES * GROUPS * (k - 1) + GROUPS * (j + 1))
                act.wait_ge(turned, TILES * NT * k + NT * j + i + 1)
                first, n = turns(k, j)[i]
                dst = feats[:, j * TILE:(j + 1) * TILE, first:first + n].rearrange("p s f -> p f s")
                copy(dst, ps_t[:, 0:n, :]).then_inc(turned_copied, 1)
                if more:
                    stage_ids(k + 1, j, i)

            def stage_ids(k, j, i):
                first, n = turns(CHUNKS - 1, j)[i]
                act.activation(ids_now[:, j, first:first + n],
                               ids_all[:, bass.ds((k * TILES + j) * NG + first, n)],
                               ACT.Copy).then_inc(ids_staged, 1)

            def relu1(m, half):
                if half == 0:
                    act.wait_ge(l2_made, 1 + m)
                act.wait_ge(l1_made, 2 * m + half + 1)
                for n in range(2):
                    out = 2 * half + n
                    act.activation(h1[:, out, :], ps_m[:, n, :], ACT.Relu,
                                   bias=b1_sb[:, out:out + 1]).then_inc(h1_made, 1)

            def last_relu1(j):
                for n in range(N1):
                    act.wait_ge(l1_made, 2 * (CHUNKS - 1) + (1 if j == 0 else n + 2))
                    act.activation(h_last[:, n, j * TILE:(j + 1) * TILE], ps_last1[j][n], ACT.Relu,
                                   bias=b1_sb[:, n:n + 1]).then_inc(h1_made, 1)

            def turn_of_loop(k, more):
                for kind, i in steps(k):
                    if kind == "select":
                        copy_selected(k, i)
                        if is_first(k) and i + RAW_AHEAD < N_SELECTED:
                            make_hi(i + RAW_AHEAD)
                    if kind == "turn0":
                        copy_turned(k, 0, i, more)
                    if kind == "turn1":
                        copy_turned(k, 1, i, more)
                    if is_first(k) and (kind, i) == ("product", 0):
                        act.wait_ge(lo_made, N_SELECTED)
                    if kind == "product":
                        copy_blocks(act, copy, k, i, (0, 1), blocks_by_act)
                    if kind == "layer1":
                        relu1(k - 1, i)
                    if kind == "last1":
                        last_relu1(i)

            act.wait_ge(ids_loaded, 16)
            for j in range(TILES):
                for i in range(NT):
                    stage_ids(0, j, i)
            for i in range(RAW_AHEAD):
                make_hi(i)
            turn_of_loop(0, True)
            act.wait_ge(weights_loaded, 16 * (KC + 4))
            turn_of_loop(1, True)
            with act.Fori(2, CHUNKS - 1) as k:
                turn_of_loop(k, True)
            turn_of_loop(CHUNKS - 1, False)

        @block.vector
        def _(dve):
            def make_one_hot(k, at):
                i, first, n = SETS[at]
                width = WIDTH[i]
                if at == 0:
                    dve.wait_ge(ids_rep_loaded, 16 * (N_SELECTED // IDS_PIECE) * (k + 1))
                at_least(dve, one_hot_used, NS * k + at - SET_RING + 1)
                rows = slice(BLOCK_AT[i] + first, BLOCK_AT[i] + first + n)
                dve.tensor_tensor(
                    one_hot[:, at % SET_RING, 0:n * width].rearrange("p (b s) -> p b s", b=n),
                    ids_rep[0:RP, i, CHUNK - width:].unsqueeze(1).broadcast_to([RP, n, width]),
                    row_id[:, rows].unsqueeze(2).broadcast_to([RP, n, width]), ALU.is_equal,
                ).then_inc(one_hot_made, 1)

            def relu2(m):
                dve.wait_ge(l3_made, 1 + m)
                dve.wait_ge(l2_made, 1 + m + 1)
                for n in range(N2):
                    dve.tensor_scalar(h2[:, n, :], ps_m[:, n, :], b2_sb[:, n:n + 1], 0.0,
                                      ALU.add, ALU.max).then_inc(h2_made, 1)

            def finish(m):
                dve.wait_ge(l3_made, 1 + m + 1)
                dve.tensor_copy(y_sb[:, bass.ds(m * TILES, TILES)], ps_m[:, 0, 0:TILES]).then_inc(y_made, 1)

            def last_relu2(j):
                dve.wait_ge(l2_made, 1 + CHUNKS + j)
                for n in range(N2):
                    dve.tensor_scalar(h_last[:, N1 + n, j * TILE:(j + 1) * TILE], ps_last2[j][n],
                                      b2_sb[:, n:n + 1], 0.0, ALU.add, ALU.max).then_inc(h2_made, 1)

            def last_finish(j):
                at = (CHUNKS - 1) * TILES + j
                dve.wait_ge(l3_made, 1 + CHUNKS + j)
                dve.tensor_copy(y_sb[:, at:at + 1], ps_last1[j][0][:, 0:1]).then_inc(y_made, 1)

            def turn_of_loop(k, more):
                if not is_first(k):
                    for at in range(AHEAD, NS - (SETS_SHARED if is_last(k) else 0)):
                        make_one_hot(k, at)
                for kind, i in steps(k):
                    if kind == "product":
                        copy_blocks(dve, dve.tensor_copy, k, i, (2, 3), blocks_by_dve)
                        if more and 0 <= i - 1 < AHEAD:
                            make_one_hot(k + 1, i - 1)
                    if kind == "layer2":
                        relu2(k - i)
                    if kind == "layer3":
                        finish(k - i)
                    if kind == "last2":
                        last_relu2(i)
                    if kind == "last3":
                        last_finish(i)

            dve.sem_inc(y_made)
            dve.memset(feats[:, :, NF:SLOT], 0.0).then_inc(pads_zeroed, 1)
            dve.wait_ge(row_ids_made, N_SELECTED)
            for i in range(N_SELECTED):
                rows = slice(BLOCK_AT[i], BLOCK_AT[i] + BLOCKS[i])
                dve.wait_ge(hi_made, i + 1)
                dve.tensor_tensor(table_lo[:, rows, :].rearrange("p b d -> p (b d)"), raw_table(i),
                                  table_hi[:, rows, :].rearrange("p b d -> p (b d)").bitcast(F32),
                                  ALU.subtract).then_inc(lo_made, 1)
                for at in range(NS):
                    if SETS[at][0] == i:
                        make_one_hot(0, at)
            dve.wait_ge(lo_made, N_SELECTED)
            turn_of_loop(0, True)
            dve.wait_ge(weights_loaded, 16 * (KC + 4))
            turn_of_loop(1, True)
            with dve.Fori(2, CHUNKS - 1) as k:
                turn_of_loop(k, True)
            turn_of_loop(CHUNKS - 1, False)


def kernel(**inputs):
    import concourse.bacc as bacc
    from concourse.bass_utils import run_bass_kernel_spmd

    def tril_row(f, g):
        a, b = max(ORDER[f], ORDER[g]), min(ORDER[f], ORDER[g])
        return a * (a - 1) // 2 + b

    x = {name: np.asarray(a) for name, a in inputs.items()}
    w1 = np.zeros((CONTRACT, H1), x["W_top1"].dtype)
    for first, n, c, p in RUNS:
        for row, (f, g) in enumerate((f, g) for f in range(first + 1, NF) for g in (first, first + 1)):
            if f != g:
                w1[c * P + p + row] = x["W_top1"][tril_row(f, g)]
    w1[PACKED:] = x["W_top1"][PAIRS:]
    laid = {
        "ids_gathered": x["ids"][:, GATHERED].reshape(BATCH // P, P, NG).transpose(1, 0, 2).reshape(P, -1),
        "ids_selected": x["ids"][:, SELECTED].T,
        "dense_t": x["dense_ctx"].T,
        "w1": w1,
        "b1": x["b_top1"].reshape(N1, P).T,
        "w2": x["W_top2"],
        "b2": x["b_top2"].reshape(N2, P).T,
        "w3": x["W_top3"].reshape(N2, P).T,
    }
    for f in range(NF):
        laid[f"tbl_{f}"] = x[f"tbl_{f}"]

    nc = bacc.Bacc("TRN2", target_bir_lowering=False, num_devices=1)
    arrays, ap = {}, {}
    for name, a in laid.items():
        arrays[f"{name}_dram"] = np.ascontiguousarray(a)
        ap[name] = nc.dram_tensor(f"{name}_dram", a.shape, mybir.dt.from_np(a.dtype), kind="ExternalInput").ap()
    y = nc.dram_tensor("y_dram", (P, BATCH // P), F32, kind="ExternalOutput").ap()
    dlrm_program(nc, ap["ids_gathered"], ap["ids_selected"], [ap[f"tbl_{f}"] for f in range(NF)],
                 ap["dense_t"], ap["w1"], ap["b1"], ap["w2"], ap["b2"], ap["w3"], y)
    done = run_bass_kernel_spmd(nc, [arrays], core_ids=[0])
    return done.results[0]["y_dram"].T.reshape(BATCH, 1)
```
